# Optimizing a Trainium2 kernel written in Bass

```python
import numpy as np
import jax
import jax.numpy as jnp

def _softmax(x, axis=-1):
    return jax.nn.softmax(x, axis=axis)

def _gelu(x):
    return jax.nn.gelu(x, approximate=True)

def _silu(x):
    return jax.nn.silu(x)

def _sigmoid(x):
    return jax.nn.sigmoid(x)

def _layernorm(x, axis=-1, eps=1e-05):
    m = jnp.mean(x, axis=axis, keepdims=True)
    v = jnp.var(x, axis=axis, keepdims=True)
    return (x - m) / jnp.sqrt(v + eps)

def _scatter_add(tgt, idx, src, axis=0):
    return tgt.at[idx].add(src)

def _segment_sum(src, seg, n):
    return jax.ops.segment_sum(src, seg, n)
kernel_name = 'mk_cond_resid_d2_seqx_r2_b89433'

def setup_inputs(seed: int=0):
    np.random.seed(seed)
    _w = jnp.asarray

    def _rec_inputs():
        import jax
        import jax.numpy as jnp
        _rk = jax.random.key(seed)
        x = -0.000125 + 0.9999 * jax.random.normal(jax.random.fold_in(_rk, 1), (32, 128, 2048), jnp.float32)
        _lenS = 128 - jax.random.randint(jax.random.fold_in(_rk, 7), (32,), 0, max(1, 128 // 4) + 1, jnp.int32)
        _lenS2 = 128 - jax.random.randint(jax.random.fold_in(_rk, 8), (32,), 0, max(1, 128 // 4) + 1, jnp.int32)
        itok_B_1_7 = jax.random.randint(jax.random.fold_in(_rk, 11), (32,), 1, 8, jnp.int32)
        itok_B_1_14 = jax.random.randint(jax.random.fold_in(_rk, 12), (32,), 1, 15, jnp.int32)
        return (x, itok_B_1_7, itok_B_1_14)
    x, itok_B_1_7, itok_B_1_14 = _rec_inputs()

    def _L0_cond_setup():
        import jax, jax.numpy as jnp
        import numpy as np
        B, S, D_IN, D_OUT = (4, 1024, 2048, 2048)
        N_ADAPTERS, MAX_RANK = (8, 16)
        key = jax.random.key(seed)
        ks = jax.random.split(key, 7)
        x = jax.random.normal(ks[0], (B, S, D_IN), dtype=jnp.float32)
        weight = jax.random.normal(ks[1], (D_OUT, D_IN), dtype=jnp.float32) * (1.0 / np.sqrt(D_IN))
        bias = jax.random.normal(ks[2], (D_OUT,), dtype=jnp.float32) * 0.01
        lora_a_weights = jax.random.normal(ks[3], (N_ADAPTERS, MAX_RANK, D_IN), dtype=jnp.float32) * (1.0 / np.sqrt(D_IN))
        lora_b_weights = jax.random.normal(ks[4], (N_ADAPTERS, D_OUT, MAX_RANK), dtype=jnp.float32) * 0.02
        scaling_factors = jax.random.uniform(ks[5], (N_ADAPTERS,), dtype=jnp.float32, minval=0.5, maxval=2.0)
        adapter_id = jax.random.randint(ks[6], (B,), 0, N_ADAPTERS, dtype=jnp.int64)
        return {'x': x, 'weight': weight, 'bias': bias, 'lora_a_weights': lora_a_weights, 'lora_b_weights': lora_b_weights, 'scaling_factors': scaling_factors, 'adapter_id': adapter_id}
    _L0_cond_all = _L0_cond_setup()
    _L0_cond_in = {k: v for k, v in _L0_cond_all.items() if k in ('weight', 'bias', 'lora_a_weights', 'lora_b_weights', 'scaling_factors')}
    del _L0_cond_all

    def _L1_cond_setup():
        import jax, jax.numpy as jnp
        import numpy as np
        B, S, D_IN = (8, 1024, 2048)
        A, D_OUT = (16, 2048)
        key = jax.random.key(seed)
        k1, k2, k3 = jax.random.split(key, 3)
        x = jax.random.normal(k1, (B, S, D_IN), dtype=jnp.float32)
        weight = jax.random.normal(k2, (A, D_OUT, D_IN), dtype=jnp.float32) * 0.02
        adapter_ids = jax.random.randint(k3, (B,), 0, A, dtype=jnp.int64)
        return {'x': x, 'weight': weight, 'adapter_ids': adapter_ids}
    _L1_cond_all = _L1_cond_setup()
    _L1_cond_in = {k: v for k, v in _L1_cond_all.items() if k in ('weight',)}
    del _L1_cond_all
    return {'x': x, 'itok_B_1_7': itok_B_1_7, 'itok_B_1_14': itok_B_1_14, 'L0_cond_weight': _L0_cond_in['weight'], 'L0_cond_bias': _L0_cond_in['bias'], 'L0_cond_lora_a_weights': _L0_cond_in['lora_a_weights'], 'L0_cond_lora_b_weights': _L0_cond_in['lora_b_weights'], 'L0_cond_scaling_factors': _L0_cond_in['scaling_factors'], 'L1_cond_weight': _L1_cond_in['weight']}

def reference(x, itok_B_1_7, itok_B_1_14, L0_cond_weight, L0_cond_bias, L0_cond_lora_a_weights, L0_cond_lora_b_weights, L0_cond_scaling_factors, L1_cond_weight):
    import jax
    import jax.numpy as jnp

    def _L0_cond_ref(x, weight, bias, lora_a_weights, lora_b_weights, scaling_factors, adapter_id):
        import jax, jax.numpy as jnp
        import numpy as np
        B, S, D_IN, D_OUT = (4, 1024, 2048, 2048)
        N_ADAPTERS, MAX_RANK = (8, 16)
        base = jnp.einsum('bsi,oi->bso', x, weight) + bias
        a_sel = lora_a_weights[adapter_id]
        b_sel = lora_b_weights[adapter_id]
        scale = scaling_factors[adapter_id]
        low = jnp.einsum('bsi,bri->bsr', x, a_sel)
        delta = jnp.einsum('bsr,bor->bso', low, b_sel)
        return base + scale[:, None, None] * delta

    def _L1_cond_ref(x, weight, adapter_ids):
        import jax, jax.numpy as jnp
        import numpy as np
        B, S, D_IN = (8, 1024, 2048)
        A, D_OUT = (16, 2048)
        w = weight[adapter_ids]
        return jnp.einsum('bij,bkj->bik', x, w)
    x = x + _L0_cond_ref(x, L0_cond_weight, L0_cond_bias, L0_cond_lora_a_weights, L0_cond_lora_b_weights, L0_cond_scaling_factors, itok_B_1_7)
    x = x + _L1_cond_ref(x, L1_cond_weight, itok_B_1_14)
    return x

_drawn_inputs = setup_inputs


def setup_inputs(seed=0):
    import zlib

    import numpy as np

    out = dict(_drawn_inputs(seed))
    spreads = {}
    factors = {'L0_cond_bias': 8.0}
    for name, (base, spread) in spreads.items():
        noise = np.random.default_rng([zlib.crc32(name.encode()), seed]).standard_normal(out[name].shape)
        drawn = base * np.exp(spread * noise) if base else spread * noise
        out[name] = jnp.asarray(drawn.astype(out[name].dtype))
    for name, factor in factors.items():
        out[name] = (out[name] * factor).astype(out[name].dtype)
    return out
```

```python
from contextlib import ExitStack

import concourse.bass as bass
from concourse import mybir

F32 = mybir.dt.float32
F32R = mybir.dt.float32r
I32 = mybir.dt.int32
ALU = mybir.AluOpType
ACT = mybir.ActivationFunctionType

P = 128
NB = 32
G = 4
NG = NB // G
T = 16
NA = 8
RANK = 16
NW = 16
C0 = T + 1
S0 = 4
C1 = 4
S1 = 8
XI = 8

R0 = 2
R1 = 3
RY = 5
RW = 4
RX = 4
BANKS = 3
NOUT = 2
LEAD = 12


def n0_of(g, c, s):
    return (g * C0 + c) * S0 + s


def n1_of(b, kc, s):
    return (b * C1 + kc) * S1 + s


def plan_blocks():
    blocks = []
    for g in range(NG + 1):
        for c in range(C0):
            first = [("L0", g, c, s, h) for s in range(S0) for h in range(2)] if g < NG else []
            second = []
            if g > 0 and c > 0:
                b, kc = (g - 1) * G + (c - 1) // C1, (c - 1) % C1
                second = [("L1", b, kc, s) for s in range(S1)]
            for i in range(max(len(first), len(second))):
                blocks += first[i:i + 1] + second[i:i + 1]
    return blocks


def plan_splits(first0, last0, first1, last1):
    splits = []

    def add(kind, index, free, need):
        splits.append((max(free + 0.5, need - LEAD), need, kind, index))

    for g in range(NG):
        for c in range(C0):
            for s in range(S0):
                n = n0_of(g, c, s)
                add("W0", (g, c, s), last0[n - R0] if n >= R0 else -1, first0[n])
        for i in range(XI):
            free = last0[n0_of(g - 1, T, i // 2)] if g else -1
            add("X", (g, i), free, first0[n0_of(g, 0, i // 2)] + 0.1 * i)
        add("LOW", (g,), last0[n0_of(g, 0, S0 - 1)] + 0.2, first0[n0_of(g, 1, 2)])
    for b in range(NB):
        g = b // G
        for kc in range(C1):
            for s in range(S1):
                n = n1_of(b, kc, s)
                add("W1", (b, kc, s), last1[n - R1] if n >= R1 else -1, first1[n])
        for u in range(4):
            made = last0[n0_of(g, 4 * u + 4, S0 - 1)] + 0.2
            v = 4 * b + u - RY
            free = last1[n1_of(v // 4, C1 - 1, 2 * (v % 4) + 1)] if v >= 0 else -1
            add("Y", (b, u), max(made, free), first1[n1_of(b, 0, 2 * u)])
    for i in range(2):
        add("B", (i,), -1, first0[n0_of(0, 0, 3)])
    splits.sort()
    return splits


def program(nc, xt, a0, w0, w1, bt, bias, ids, idsb, acol, scol, eye, out):
    blocks = plan_blocks()
    first0, last0, first1, last1 = {}, {}, {}, {}
    for at, block in enumerate(blocks):
        if block[0] == "L0":
            n = n0_of(*block[1:4])
            first0.setdefault(n, at)
            last0[n] = at
        else:
            n = n1_of(*block[1:4])
            first1[n] = last1[n] = at
    splits = plan_splits(first0, last0, first1, last1)
    number = {(kind, *index): n for n, (_, _, kind, index) in enumerate(splits)}

    with ExitStack() as ctx:
        def sb(name, shape, dt=F32):
            return ctx.enter_context(nc.sbuf_tensor(name, shape, dt))

        def sem(name):
            return ctx.enter_context(nc.semaphore(name))

        xh = sb("xh", [P, T, G * P], F32R)
        xl = sb("xl", [P, T, G * P], F32R)
        ybuf = sb("ybuf", [P, T * G * P])
        yh = sb("yh", [P, RY, 4, P], F32R)
        yl = sb("yl", [P, RY, 4, P], F32R)
        w0h = sb("w0h", [P, R0, 4, P], F32R)
        w0l = sb("w0l", [P, R0, 4, P], F32R)
        w1h = sb("w1h", [P, R1, 2, 512], F32R)
        w1l = sb("w1l", [P, R1, 2, 512], F32R)
        bh = sb("bh", [P, T, P], F32R)
        bl = sb("bl", [P, T, P], F32R)
        low = sb("low", [P, G * P])
        lowh = sb("lowh", [P, G * P], F32R)
        lowl = sb("lowl", [P, G * P], F32R)
        wraw = sb("wraw", [P, RW, 1024])
        xraw = sb("xraw", [P, RX, 1024])
        ost = sb("ost", [P, NOUT, 512])
        eye_s = sb("eye_s", [P, P])
        bias_s = sb("bias_s", [P, T])
        idsb_i = sb("idsb_i", [P, NB], I32)
        idsb_f = sb("idsb_f", [P, NB])
        mask = sb("mask", [P, NB])
        cols = sb("cols", [P, 2])
        acc0 = [ctx.enter_context(nc.psum_tensor(f"acc0_{i}", [P, 512], F32)) for i in range(BANKS)]
        acc1 = [ctx.enter_context(nc.psum_tensor(f"acc1_{i}", [P, 512], F32)) for i in range(BANKS)]

        s_const = sem("s_const")
        s_eye = sem("s_eye")
        s_idf = sem("s_idf")
        s_mask = sem("s_mask")
        s_wraw = [sem(f"s_wraw{i}") for i in range(RW)]
        s_xraw = [sem(f"s_xraw{i}") for i in range(RX)]
        s_diag = sem("s_diag")
        s_hi = sem("s_hi")
        s_lo = sem("s_lo")
        s_w0 = sem("s_w0")
        s_w1 = sem("s_w1")
        s_ev0 = sem("s_ev0")
        s_ev1 = sem("s_ev1")
        s_out = [sem(f"s_out{i}") for i in range(NOUT)]

        strides = [(16, 4, 1)]
        for _ in range(NG - 1):
            o1, o0, b = strides[-1]
            strides.append((b, o1, o0))

        def y_view(g):
            names = dict(zip(strides[g], ("o1", "o0", "b")))
            v = ybuf[:, :].rearrange(f"p ({names[16]} {names[4]} {names[1]} t) -> p o1 o0 b t",
                                     o1=4, o0=4, b=4, t=P)
            return v

        place, turn, before, diag_count = {}, {}, {}, {}
        rings = {"W0": (RW, []), "W1": (RW, None), "B": (RW, None), "X": (RX, [])}
        wlist, xlist = rings["W0"][1], rings["X"][1]
        diagonals = 0
        for n, (_, _, kind, index) in enumerate(splits):
            if kind in ("Y", "LOW"):
                continue
            ring, size = (xlist, RX) if kind == "X" else (wlist, RW)
            k = len(ring)
            place[n], turn[n] = k % size, k // size + 1
            before[n] = ring[k - size] if k >= size else None
            ring.append(n)
            if diag_blocks(kind, index):
                diagonals += 1
                diag_count[n] = diagonals

        def raw_of(n):
            kind = splits[n][2]
            if kind == "X":
                return xraw[:, place[n], :]
            return wraw[:, place[n], 0:512 if kind == "W0" else 1024]

        def raw_sem(n):
            return (s_xraw if splits[n][2] == "X" else s_wraw)[place[n]]

        loads = []
        for n in sorted(place):
            kind, index = splits[n][2:4]
            key = before[n] + 0.5 if before[n] is not None else -1
            if kind == "X" and index[0] and index[1] < RX:
                key = number["W0", index[0] - 1, 6 + 2 * index[1], 0] + 0.5
            loads.append((key, n))
        loads.sort()

        scalar_tasks, vector_tasks = [], []
        for n, (key, _, kind, index) in enumerate(splits):
            scalar_tasks.append((key, n, "hi", index))
            vector_tasks.append((key, n, "lo", index))
        for i in range(NG * C0):
            vector_tasks.append((last0[S0 * i + S0 - 1] + 0.6, i, "ev0", (i // C0, i % C0)))
        for i in range(NB * C1):
            at = last1[S1 * i + S1 - 1]
            scalar_tasks.append((at + 0.6, i, "ev1", None))
            scalar_tasks.append((at + 2.1, i, "store", None))
        scalar_tasks.sort(key=lambda t: t[:2])
        vector_tasks.sort(key=lambda t: t[:2])

        block = ctx.enter_context(nc.Block())

        @block.sync
        def _(eng):
            eng.dma_start(eye_s[:], eye).then_inc(s_eye, 16)
            ident = {}
            started = False
            for _, n in loads:
                kind, index = splits[n][2:4]
                if before[n] is not None:
                    eng.wait_ge(s_lo, before[n] + 1)
                dst = raw_of(n)
                if kind == "X":
                    src = xt[index[0], index[1]]
                elif kind == "B":
                    src = bt[:, index[0] * 1024:(index[0] + 1) * 1024]
                elif kind == "W0":
                    g, c, s = index
                    src = a0[s] if c == 0 else w0[c - 1, s]
                else:
                    b, kc, s = index
                    if b not in ident:
                        ident.clear()
                        ident[b] = eng.value_load(ids[0:1, b:b + 1], min_val=0, max_val=NW - 1)
                    src = w1[bass.ds(ident[b], 1), kc, s].rearrange("a p n -> (a p) n")
                eng.dma_start(dst, src).then_inc(raw_sem(n), 16)
                if not started and n >= 6:
                    started = True
                    eng.dma_start(bias_s[:], bias).then_inc(s_const, 16)
                    eng.dma_start(idsb_i[:], idsb).then_inc(s_const, 16)
                    eng.dma_start(cols[:, 0:1], acol).then_inc(s_const, 16)
                    eng.dma_start(cols[:, 1:2], scol).then_inc(s_const, 16)

        @block.gpsimd
        def _(eng):
            eng.wait_ge(s_eye, 16)
            for n in sorted(diag_count):
                kind, index = splits[n][2:4]
                eng.wait_ge(raw_sem(n), 16 * turn[n])
                cuts = diag_blocks(kind, index)
                for at in cuts:
                    v = wraw[:, place[n], at:at + P]
                    ins = eng.tensor_tensor(v, v, eye_s[:], ALU.add)
                ins.then_inc(s_diag, 1)

        def split_views(n):
            kind, index = splits[n][2:4]
            if kind == "X":
                i = index[1]
                v = raw_of(n).rearrange("p (t n) -> p t n", t=2)
                return v, xh[:, 2 * i:2 * i + 2, :], xl[:, 2 * i:2 * i + 2, :]
            if kind == "B":
                i = index[0]
                v = raw_of(n).rearrange("p (t n) -> p t n", t=8)
                return v, bh[:, 8 * i:8 * i + 8, :], bl[:, 8 * i:8 * i + 8, :]
            if kind == "W0":
                k = n0_of(*index) % R0
                v = raw_of(n).rearrange("p (t n) -> p t n", t=4)
                return v, w0h[:, k], w0l[:, k]
            if kind == "W1":
                k = n1_of(*index) % R1
                v = raw_of(n).rearrange("p (t n) -> p t n", t=2)
                return v, w1h[:, k], w1l[:, k]
            if kind == "Y":
                b, u = index
                k = (4 * b + u) % RY
                return y_view(b // G)[:, u, :, b % G, :], yh[:, k], yl[:, k]
            return low[:], lowh[:], lowl[:]

        @block.scalar
        def _(eng):
            for _, n, what, index in scalar_tasks:
                if what == "ev1":
                    if n >= NOUT:
                        eng.wait_ge(s_out[n % NOUT], 16 * (n // NOUT))
                    eng.wait_ge(s_w1, S1 * (n + 1))
                    eng.copy(ost[:, n % NOUT, :], acc1[n % BANKS][:]).then_inc(s_ev1, 1)
                    continue
                if what == "store":
                    b, kc = n // C1, n % C1
                    eng.wait_ge(s_ev1, n + 1)
                    eng.dma_start(out[b, :, kc * 512:(kc + 1) * 512], ost[:, n % NOUT, :])\
                        .then_inc(s_out[n % NOUT], 16)
                    continue
                kind = splits[n][2]
                if kind in ("X", "B", "W0", "W1"):
                    if n in diag_count:
                        eng.wait_ge(s_diag, diag_count[n])
                    else:
                        eng.wait_ge(raw_sem(n), 16 * turn[n])
                if kind == "X" and index[0]:
                    eng.wait_ge(s_w0, n0_of(index[0] - 1, T, index[1] // 2) + 1)
                elif kind == "W0" and n0_of(*index) >= R0:
                    eng.wait_ge(s_w0, n0_of(*index) - R0 + 1)
                elif kind == "W1" and n1_of(*index) >= R1:
                    eng.wait_ge(s_w1, n1_of(*index) - R1 + 1)
                elif kind == "Y":
                    b, u = index
                    eng.wait_ge(s_ev0, (b // G) * C0 + 4 * u + 5)
                    v = 4 * b + u - RY
                    if v >= 0:
                        eng.wait_ge(s_w1, n1_of(v // 4, C1 - 1, 2 * (v % 4) + 1) + 1)
                elif kind == "LOW":
                    g = index[0]
                    eng.wait_ge(s_ev0, g * C0 + 1)
                    if g:
                        eng.wait_ge(s_w0, n0_of(g - 1, T, 2) + 1)
                src, hi, _ = split_views(n)
                eng.copy(hi, src).then_inc(s_hi, 1)
            for k in range(NOUT):
                eng.wait_ge(s_out[k], 16 * (NB * C1 // NOUT))

        @block.vector
        def _(eng):
            eng.wait_ge(s_const, 64)
            eng.tensor_copy(idsb_f[:], idsb_i[:]).then_inc(s_idf, 1)
            eng.wait_ge(s_idf, 1)
            eng.tensor_scalar(mask[:], idsb_f[:], cols[:, 0:1], cols[:, 1:2], ALU.is_equal, ALU.mult)\
                .then_inc(s_mask, 1)
            eng.wait_ge(s_mask, 1)
            for _, n, what, index in vector_tasks:
                if what == "ev0":
                    g, c = index
                    eng.wait_ge(s_w0, S0 * (n + 1))
                    acc = acc0[n % BANKS][:].rearrange("p (b t) -> p b t", b=G)
                    if c == 0:
                        if g:
                            eng.wait_ge(s_lo, number["LOW", g - 1] + 1)
                        m = mask[:, G * g:G * (g + 1)].unsqueeze(2).to_broadcast([P, G, P])
                        eng.tensor_tensor(low[:].rearrange("p (b t) -> p b t", b=G), acc, m, ALU.mult)\
                            .then_inc(s_ev0, 1)
                    else:
                        o = c - 1
                        if g and o % 4 == 0:
                            eng.wait_ge(s_lo, max(number["Y", (g - 1) * G + o // 4, u] for u in range(4)) + 1)
                        eng.tensor_scalar(y_view(g)[:, o // 4, o % 4, :, :], acc, bias_s[:, o:o + 1], None,
                                          ALU.add).then_inc(s_ev0, 1)
                    continue
                eng.wait_ge(s_hi, n + 1)
                src, hi, lo = split_views(n)
                eng.tensor_tensor(lo, src, hi, ALU.subtract).then_inc(s_lo, 1)

        @block.tensor
        def _(eng):
            for blk in blocks:
                if blk[0] == "L0":
                    _, g, c, s, half = blk
                    i, n = g * C0 + c, n0_of(g, c, s)
                    acc = acc0[i % BANKS][:]
                    if s == 0 and half == 0 and i >= BANKS:
                        eng.wait_ge(s_ev0, i - BANKS + 1)
                    if c > 0 and s == 2 and half == 0:
                        if c == 1:
                            eng.wait_ge(s_lo, max(number["LOW", g], number["B", 0], number["B", 1]) + 1)
                        for a, m in ((bh, lowh), (bh, lowl), (bl, lowh)):
                            eng.matmul(acc, a[:, c - 1, :], m[:], start=False, stop=False)
                    if half == 0:
                        eng.wait_ge(s_lo, number["W0", g, c, s] + 1)
                    for t in range(2 * half, 2 * half + 2):
                        j = 4 * s + t
                        if c == 0 and j % 2 == 0:
                            eng.wait_ge(s_lo, number["X", g, j // 2] + 1)
                        wh, wl = w0h[:, n % R0, t, :], w0l[:, n % R0, t, :]
                        for a, m in ((wh, xh), (wh, xl), (wl, xh)):
                            ins = eng.matmul(acc, a, m[:, j, :], start=(j == 0 and a is wh and m is xh),
                                             stop=(j == T - 1 and a is wl))
                    if half == 1:
                        ins.then_inc(s_w0, 1)
                else:
                    _, b, kc, s = blk
                    i, n = b * C1 + kc, n1_of(b, kc, s)
                    acc = acc1[i % BANKS][:]
                    if s == 0 and i >= BANKS:
                        eng.wait_ge(s_ev1, i - BANKS + 1)
                    if kc == 0 and s % 2 == 0:
                        eng.wait_ge(s_lo, number["Y", b, s // 2] + 1)
                    eng.wait_ge(s_lo, number["W1", b, kc, s] + 1)
                    for t in range(2):
                        j = 2 * s + t
                        k = (4 * b + j // 4) % RY
                        ah, al = yh[:, k, j % 4, :], yl[:, k, j % 4, :]
                        wh, wl = w1h[:, n % R1, t, :], w1l[:, n % R1, t, :]
                        for a, m in ((ah, wh), (ah, wl), (al, wh)):
                            ins = eng.matmul(acc, a, m, start=(j == 0 and a is ah and m is wh),
                                             stop=(j == T - 1 and a is al))
                    ins.then_inc(s_w1, 1)


def diag_blocks(kind, index):
    if kind == "W0":
        _, c, s = index
        return [((c - 1) % 4) * P] if c > 0 and (c - 1) // 4 == s else []
    if kind == "W1":
        _, kc, s = index
        return [512 * (t % 2) + P * (t % 4) for t in (2 * s, 2 * s + 1)] if s // 2 == kc else []
    return []


def kernel(x, itok_B_1_7, itok_B_1_14, L0_cond_weight, L0_cond_bias, L0_cond_lora_a_weights,
           L0_cond_lora_b_weights, L0_cond_scaling_factors, L1_cond_weight):
    import numpy as np
    import concourse.bacc as bacc
    from concourse.bass_utils import run_bass_kernel_spmd as run

    c = np.ascontiguousarray
    x = np.asarray(x)
    arrays = {
        "xt": c(x.reshape(NG, G * P, XI, 2, P).transpose(0, 2, 4, 3, 1)).reshape(NG, XI, P, 1024),
        "a0": c(np.asarray(L0_cond_lora_a_weights).reshape(NA * RANK, S0, 4, P).transpose(1, 3, 2, 0))
        .reshape(S0, P, 512),
        "w0": c(np.asarray(L0_cond_weight).reshape(T, P, S0, 4, P).transpose(0, 2, 4, 3, 1)).reshape(T, S0, P, 512),
        "w1": c(np.asarray(L1_cond_weight).reshape(NW, C1, 512, S1, 2, P).transpose(0, 1, 3, 5, 4, 2))
        .reshape(NW, C1, S1, P, 1024),
        "bt": c(np.asarray(L0_cond_lora_b_weights).transpose(0, 2, 1)).reshape(P, T * P),
        "bias": c(np.asarray(L0_cond_bias).reshape(T, P).T),
        "ids": c(np.asarray(itok_B_1_14).reshape(1, NB)),
        "idsb": c(np.broadcast_to(np.asarray(itok_B_1_7).reshape(1, NB), (P, NB))),
        "acol": c((np.arange(P) // RANK).astype(np.float32).reshape(P, 1)),
        "scol": c(np.repeat(np.asarray(L0_cond_scaling_factors), RANK).reshape(P, 1)),
        "eye": np.eye(P, dtype=np.float32),
    }
    nc = bacc.Bacc("TRN2", target_bir_lowering=False, num_devices=1)
    aps = {name: nc.dram_tensor(name, a.shape, mybir.dt.from_np(a.dtype), kind="ExternalInput").ap()
           for name, a in arrays.items()}
    o = nc.dram_tensor("out", (NB, P, T * P), F32, kind="ExternalOutput").ap()
    program(nc, **aps, out=o)
    r = run(nc, [arrays], core_ids=[0])
    return r.results[0]["out"]
```

```python
from contextlib import ExitStack

import concourse.bass as bass
from concourse import mybir

F32 = mybir.dt.float32
F32R = mybir.dt.float32r
I32 = mybir.dt.int32
ALU = mybir.AluOpType
ACT = mybir.ActivationFunctionType

P = 128
NB = 32
G = 4
SIZES = [4] * 8
NG = len(SIZES)
FIRST = [sum(SIZES[:g]) for g in range(NG)]
PAIRS = [n // 2 for n in SIZES]
GROUP = [g for g in range(NG) for _ in range(SIZES[g])]
N2 = 2 * 128
T = 16
NA = 8
RANK = 16
NW = 16
C0 = T + 1
S0 = 4
SA = 2
BSLOT = 3
C1 = 4
S1 = 8
XI = 8

R0 = 2
R1 = 3
RY = 5
RW = 5
RX = 3
BANKS = 3
NOUT = 2
LEAD = 12


def n0_of(g, c, s):
    return g * (SA + T * S0) + (SA + (c - 1) * S0 if c else 0) + s


def n1_of(b, kc, s):
    return (b * C1 + kc) * S1 + s


def plan_blocks():
    blocks = []
    for g in range(NG + 1):
        first = [("L0", g, c, s, h) for c in range(C0) for s in range(S0 if c else SA) for h in range(2)]
        batches = range(FIRST[g - 1], FIRST[g - 1] + SIZES[g - 1]) if g else []
        second = [("L1", b, kc, s) for b in batches for kc in range(C1) for s in range(S1)]
        alone, rest = (first[:2 * SA], first[2 * SA:]) if g < NG else ([], [])
        blocks += alone
        done = 0
        for i in range(len(rest)):
            blocks.append(rest[i])
            until = (i + 1) * len(second) // len(rest)
            blocks += second[done:until]
            done = until
        blocks += second[done:]
    return blocks


def plan_splits(first0, last0, first1, last1):
    splits = []

    def add(kind, index, free, need):
        splits.append((max(free + 0.5, need - LEAD), need, kind, index))

    for g in range(NG):
        for c in range(C0):
            for s in range(S0 if c else SA):
                n = n0_of(g, c, s)
                add("W0", (g, c, s), last0[n - R0] if n >= R0 else -1, first0[n] + (0 if c else 0.15))
        for i in range(XI):
            free = last0[n0_of(g - 1, T, i // 2)] if g else -1
            add("X", (g, i), free, first0[n0_of(g, 0, i // 4)] + 0.1 * i)
        add("LOW", (g,), last0[n0_of(g, 0, SA - 1)] + 0.2, first0[n0_of(g, 1, BSLOT)])
        for q in range(PAIRS[g]):
            at = last0[n0_of(g - 1, 10 + q, 0)] if g else last0[n0_of(0, 1, q)] + 0.1
            splits.append((at + 0.5, first0[n0_of(g, 1, BSLOT)], "B", (g, q, 0)))
            at = first0[n0_of(g, 3 + q, 0)]
            splits.append((at + 0.5, first0[n0_of(g, 9, BSLOT)], "B", (g, q, 1)))
    for b in range(NB):
        g = GROUP[b]
        for kc in range(C1):
            for s in range(S1):
                n = n1_of(b, kc, s)
                add("W1", (b, kc, s), last1[n - R1] if n >= R1 else -1, first1[n])
        for u in range(4):
            made = last0[n0_of(g, 4 * u + 4, S0 - 1)] + 0.2
            v = 4 * b + u - RY
            free = last1[n1_of(v // 4, C1 - 1, 2 * (v % 4) + 1)] if v >= 0 else -1
            add("Y", (b, u), max(made, free), first1[n1_of(b, 0, 2 * u)])
    splits.sort()
    return splits


def program(nc, xt, a0, w0, w1, bt, bias, ids, ids0, idsb, half, scal, eye, out):
    blocks = plan_blocks()
    first0, last0, first1, last1 = {}, {}, {}, {}
    for at, block in enumerate(blocks):
        if block[0] == "L0":
            n = n0_of(*block[1:4])
            first0.setdefault(n, at)
            last0[n] = at
        else:
            n = n1_of(*block[1:4])
            first1[n] = last1[n] = at
    splits = plan_splits(first0, last0, first1, last1)
    number = {(kind, *index): n for n, (_, _, kind, index) in enumerate(splits)}

    with ExitStack() as ctx:
        def sb(name, shape, dt=F32):
            return ctx.enter_context(nc.sbuf_tensor(name, shape, dt))

        def sem(name):
            return ctx.enter_context(nc.semaphore(name))

        xh = sb("xh", [P, T, G * P], F32R)
        xl = sb("xl", [P, T, G * P], F32R)
        ybuf = sb("ybuf", [P, T * G * P])
        yh = sb("yh", [P, RY, 4, P], F32R)
        yl = sb("yl", [P, RY, 4, P], F32R)
        w0s = sb("w0s", [P, R0, 2, 4, P], F32R)
        w1h = sb("w1h", [P, R1, 2, 512], F32R)
        w1l = sb("w1l", [P, R1, 2, 512], F32R)
        bs = sb("bs", [P, 2, T * P], F32R)
        low = sb("low", [32, G * P])
        lows = sb("lows", [P, G * P], F32R)
        wraw = sb("wraw", [P, RW, 1024])
        xraw = sb("xraw", [P, RX, 1024])
        ost = sb("ost", [P, NOUT, 512])
        eye_s = sb("eye_s", [P, P])
        bias_s = sb("bias_s", [P, T])
        idsb_i = sb("idsb_i", [P, NB], I32)
        idsb_f = sb("idsb_f", [P, NB])
        mask = sb("mask", [P, NB])
        part = sb("part", [P, NB])
        half_s = sb("half_s", [P, NB])
        scal_s = sb("scal_s", [P, NA])
        acc0 = [ctx.enter_context(nc.psum_tensor(f"acc0_{i}", [P, 512], F32)) for i in range(BANKS)]
        acc1 = [ctx.enter_context(nc.psum_tensor(f"acc1_{i}", [P, 512], F32)) for i in range(BANKS)]

        acca = ctx.enter_context(nc.psum_tensor("acca", [P, 512], F32))

        s_const = sem("s_const")
        s_eye = sem("s_eye")
        s_mask = sem("s_mask")
        s_wraw = [sem(f"s_wraw{i}") for i in range(RW)]
        s_xraw = [sem(f"s_xraw{i}") for i in range(RX)]
        s_diag = sem("s_diag")
        s_hi = sem("s_hi")
        s_lo = sem("s_lo")
        s_w0 = sem("s_w0")
        s_w1 = sem("s_w1")
        s_ev0 = sem("s_ev0")
        s_low = sem("s_low")
        s_ev1 = sem("s_ev1")
        s_out = [sem(f"s_out{i}") for i in range(NOUT)]

        strides = [(16, 4, 1)]
        for _ in range(NG - 1):
            o1, o0, b = strides[-1]
            strides.append((b, o1, o0))

        def quarter(g, o1):
            return (o1 + 2) % 4 if g and SIZES[g - 1] == 2 else o1

        def y_view(g):
            names = dict(zip(strides[g], ("o1", "o0", "b")))
            v = ybuf[:, :].rearrange(f"p ({names[16]} {names[4]} {names[1]} t) -> p o1 o0 b t",
                                     o1=4, o0=4, b=4, t=P)
            return v

        place, landed, before, diag_count = {}, {}, {}, {}
        wlist, xlist = [], []
        diagonals = 0
        for n, (_, _, kind, index) in enumerate(splits):
            if kind in ("Y", "LOW"):
                continue
            ring, size = (xlist, RX) if kind in ("X", "B") else (wlist, RW)
            k = len(ring)
            place[n] = k % size
            before[n] = ring[k - size] if k >= size else None
            landed[n] = (landed[before[n]] if k >= size else 0) + 16 * transfers(kind, index)
            ring.append(n)
            if diag_blocks(kind, index):
                diagonals += 1
                diag_count[n] = diagonals

        def raw_of(n):
            kind = splits[n][2]
            size = SIZES[splits[n][3][0]] if kind != "W1" else 0
            if kind == "X":
                return xraw[:, place[n], 0:2 * P * size]
            if kind == "B":
                return xraw[0:2 * RANK, place[n], :]
            if kind == "W0" and splits[n][3][1] == 0:
                return wraw[:, place[n], 0:8 * RANK * size]
            return wraw[:, place[n], 0:512 if kind == "W0" else 1024]

        def raw_sem(n):
            return (s_xraw if splits[n][2] in ("X", "B") else s_wraw)[place[n]]

        loads = []
        for n in sorted(place):
            kind, index = splits[n][2:4]
            key = before[n] + 0.5 if before[n] is not None else -1
            if kind == "X" and index[0] and index[1] < RX:
                key = max(key, number["W0", index[0] - 1, 12 + index[1], 0] + 0.5)
            loads.append((key, n))
        loads.sort()

        scalar_tasks, vector_tasks = [], []
        for n, (key, _, kind, index) in enumerate(splits):
            scalar_tasks.append((key, n, "hi", index))
            vector_tasks.append((key, n, "lo", index))
        vector_tasks.append((3, 0, "mask", None))
        for g in range(NG):
            vector_tasks.append((last0[n0_of(g, 0, SA - 1)] + 0.6, g, "low", None))
            for o in range(T):
                vector_tasks.append((last0[n0_of(g, o + 1, S0 - 1)] + 0.6, g * T + o, "ev0", (g, o)))
        for i in range(NB * C1):
            at = last1[S1 * i + S1 - 1]
            scalar_tasks.append((at + 0.6, i, "ev1", None))
            scalar_tasks.append((at + 2.1, i, "store", None))
        scalar_tasks.sort(key=lambda t: t[:2])
        vector_tasks.sort(key=lambda t: t[:2])

        block = ctx.enter_context(nc.Block())

        @block.sync
        def _(eng):
            ids_of = {}

            def adapters(g):
                if g not in ids_of:
                    ids_of.pop(g - 2, None)
                    span = slice(FIRST[g], FIRST[g] + SIZES[g])
                    for table, top in ((ids0, NA), (ids, NW)):
                        _, values = nc.values_load_multi_w_load_instructions(
                            table[0:1, span], engines=[mybir.EngineType.SP], min_val=0, max_val=top - 1)
                        ids_of.setdefault(g, []).append(values)
                return ids_of[g]

            started = False
            for _, n in loads:
                kind, index = splits[n][2:4]
                if before[n] is not None:
                    eng.wait_ge(s_lo, before[n] + 1)
                dst = raw_of(n)
                if kind == "W0" and index[1] == 0:
                    g, _, s = index
                    for i in range(SIZES[g]):
                        src = a0[bass.ds(adapters(g)[0][i], 1), s].rearrange("a p n -> (a p) n")
                        eng.dma_start(dst[:, P * i:P * i + P], src).then_inc(raw_sem(n), 16)
                    continue
                if kind == "B":
                    g, q, h = index
                    for i in range(2):
                        src = bt[bass.ds(adapters(g)[0][2 * q + i], 1), :, h * 1024:(h + 1) * 1024]
                        eng.dma_start(dst[RANK * i:RANK * (i + 1)], src.rearrange("a r n -> (a r) n"))\
                            .then_inc(raw_sem(n), 16)
                    continue
                if kind == "X":
                    g, i = index
                    src = x_rows(xt, g, i)
                elif kind == "W0":
                    g, c, s = index
                    src = w0[c - 1, s]
                else:
                    b, kc, s = index
                    own = adapters(GROUP[b])[1][b - FIRST[GROUP[b]]]
                    src = w1[bass.ds(own, 1), kc, s].rearrange("a p n -> (a p) n")
                if kind == "X":
                    dst = dst.rearrange("p (t n) -> p t n", t=2)
                    src = src if SIZES[g] < G else src.rearrange("p (t n) -> p t n", t=2)
                eng.dma_start(dst, src).then_inc(raw_sem(n), 16)
                if not started and n >= 6:
                    started = True
                    eng.dma_start(eye_s[:], eye).then_inc(s_eye, 16)
                    eng.dma_start(bias_s[:], bias).then_inc(s_const, 16)
                    eng.dma_start(idsb_i[:], idsb).then_inc(s_const, 16)
                    eng.dma_start(half_s[:], half).then_inc(s_const, 16)
                    eng.dma_start(scal_s[:], scal).then_inc(s_const, 16)

        @block.gpsimd
        def _(eng):
            eng.wait_ge(s_eye, 16)
            for n in sorted(diag_count):
                kind, index = splits[n][2:4]
                eng.wait_ge(raw_sem(n), landed[n])
                cuts = diag_blocks(kind, index)
                for at in cuts:
                    v = wraw[:, place[n], at:at + P]
                    ins = eng.tensor_tensor(v, v, eye_s[:], ALU.add)
                ins.then_inc(s_diag, 1)

        def a_view(k):
            return w0s[:, k].rearrange("p h t n -> p (h t) n")

        def split_views(n):
            kind, index = splits[n][2:4]
            if kind == "X":
                g, i = index
                v = raw_of(n).rearrange("p (t n) -> p t n", t=2)
                hi, lo = (w[:, 2 * i:2 * i + 2, 0:P * SIZES[g]] for w in (xh, xl))
            elif kind == "B":
                _, q, h = index
                src, dst = raw_of(n), bs[:, q, 1024 * h:1024 * (h + 1)]
                return ([(src, dst[0:32]), (src, dst[32:64])],
                        [(src, None, dst[96:128]), (src, dst[0:32], dst[64:96])])
            elif kind == "W0" and index[1] == 0:
                g = index[0]
                v = raw_of(n).rearrange("p (b t r) -> p t b r", t=8, r=RANK)
                dst = a_view(n0_of(*index) % R0).rearrange("p t (b r) -> p t b r", r=RANK)
                hi, lo = dst[:, :, 0:SIZES[g]], dst[:, :, 4:4 + SIZES[g]]
            elif kind == "W0":
                k = n0_of(*index) % R0
                v, hi, lo = raw_of(n).rearrange("p (t n) -> p t n", t=4), w0s[:, k, 0], w0s[:, k, 1]
            elif kind == "W1":
                k = n1_of(*index) % R1
                v, hi, lo = raw_of(n).rearrange("p (t n) -> p t n", t=2), w1h[:, k], w1l[:, k]
            elif kind == "Y":
                b, u = index
                g, k = GROUP[b], (4 * b + u) % RY
                v, hi, lo = y_view(g)[:, quarter(g, u), :, b - FIRST[g], :], yh[:, k], yl[:, k]
            else:
                n = P * SIZES[index[0]]
                src, dst = low[:, 0:n], lows[:, 0:n]
                return [(src, dst[0:32]), (src, dst[64:96])], [(src, dst[0:32], dst[32:64])]
            return [(v, hi)], [(v, hi, lo)]

        @block.scalar
        def _(eng):
            for _, n, what, index in scalar_tasks:
                if what == "ev1":
                    if n >= NOUT:
                        eng.wait_ge(s_out[n % NOUT], 16 * (n // NOUT))
                    eng.wait_ge(s_w1, S1 * (n + 1))
                    eng.copy(ost[:, n % NOUT, :], acc1[n % BANKS][:]).then_inc(s_ev1, 1)
                    continue
                if what == "store":
                    b, kc = n // C1, n % C1
                    eng.wait_ge(s_ev1, n + 1)
                    eng.dma_start(out[b, :, kc * 512:(kc + 1) * 512], ost[:, n % NOUT, :])\
                        .then_inc(s_out[n % NOUT], 16)
                    continue
                kind = splits[n][2]
                if kind in ("X", "B", "W0", "W1"):
                    if n in diag_count:
                        eng.wait_ge(s_diag, diag_count[n])
                    else:
                        eng.wait_ge(raw_sem(n), landed[n])
                if kind == "X" and index[0]:
                    eng.wait_ge(s_w0, n0_of(index[0] - 1, T, index[1] // 2) + 1)
                elif kind == "W0" and n0_of(*index) >= R0:
                    eng.wait_ge(s_w0, n0_of(*index) - R0 + 1)
                elif kind == "W1" and n1_of(*index) >= R1:
                    eng.wait_ge(s_w1, n1_of(*index) - R1 + 1)
                elif kind == "Y":
                    b, u = index
                    eng.wait_ge(s_ev0, GROUP[b] * T + 4 * u + 4)
                    v = 4 * b + u - RY
                    if v >= 0:
                        eng.wait_ge(s_w1, n1_of(v // 4, C1 - 1, 2 * (v % 4) + 1) + 1)
                elif kind == "LOW":
                    g = index[0]
                    eng.wait_ge(s_low, g + 1)
                    if g:
                        eng.wait_ge(s_w0, n0_of(g - 1, T, BSLOT) + 1)
                if kind == "B" and index[0]:
                    eng.wait_ge(s_w0, n0_of(index[0] - 1, 8 + 8 * index[2], BSLOT) + 1)
                for src, hi in split_views(n)[0]:
                    ins = eng.copy(hi, src)
                ins.then_inc(s_hi, 1)
            for k in range(NOUT):
                eng.wait_ge(s_out[k], 16 * (NB * C1 // NOUT))

        @block.vector
        def _(eng):
            for _, n, what, index in vector_tasks:
                if what == "mask":
                    eng.wait_ge(s_const, 64)
                    eng.tensor_copy(idsb_f[:], idsb_i[:]).then_inc(s_mask, 1)
                    eng.wait_ge(s_mask, 1)
                    eng.tensor_scalar(mask[:], idsb_f[:], 0.0, scal_s[:, 0:1], ALU.is_equal, ALU.mult)\
                        .then_inc(s_mask, 1)
                    for a in range(1, NA):
                        eng.tensor_scalar(part[:], idsb_f[:], float(a), scal_s[:, a:a + 1], ALU.is_equal,
                                          ALU.mult).then_inc(s_mask, 1)
                        eng.wait_ge(s_mask, 2 * a + 1)
                        eng.tensor_tensor(mask[:], mask[:], part[:], ALU.add).then_inc(s_mask, 1)
                        eng.wait_ge(s_mask, 2 * a + 2)
                    eng.tensor_tensor(mask[:], mask[:], half_s[:], ALU.mult).then_inc(s_mask, 1)
                    eng.wait_ge(s_mask, 2 * NA + 1)
                    continue
                if what == "low":
                    eng.wait_ge(s_w0, n0_of(n, 0, SA - 1) + 1)
                    if n:
                        eng.wait_ge(s_lo, number["LOW", n - 1] + 1)
                        eng.wait_ge(s_w0, n0_of(n - 1, T, BSLOT) + 1)
                    for q in range(PAIRS[n]):
                        b, at = FIRST[n] + 2 * q, N2 * q
                        for row, dst in ((32 * q, low), (64 + 32 * q, lows[96:128])):
                            m = mask[row:row + 32, b:b + 2].unsqueeze(2).to_broadcast([32, 2, P])
                            acc = acca[row:row + 32, at:at + N2].rearrange("p (b t) -> p b t", b=2)
                            ins = eng.tensor_tensor(dst[:, at:at + N2].rearrange("p (b t) -> p b t", b=2),
                                                    acc, m, ALU.mult)
                    ins.then_inc(s_low, 1)
                    continue
                if what == "ev0":
                    g, o = index
                    size = SIZES[g]
                    eng.wait_ge(s_w0, n0_of(g, o + 1, S0 - 1) + 1)
                    if g and o % 4 == 0:
                        old = quarter(g, o // 4)
                        if old < SIZES[g - 1]:
                            eng.wait_ge(s_lo, max(number["Y", FIRST[g - 1] + old, u] for u in range(4)) + 1)
                    acc = acc0[n % BANKS][:, 0:P * size].rearrange("p (b t) -> p b t", b=size)
                    eng.tensor_scalar(y_view(g)[:, quarter(g, o // 4), o % 4, 0:size, :], acc, bias_s[:, o:o + 1],
                                      None, ALU.add).then_inc(s_ev0, 1)
                    continue
                eng.wait_ge(s_hi, n + 1)
                for src, hi, lo in split_views(n)[1]:
                    ins = eng.tensor_tensor(lo, src, hi, ALU.subtract) if hi is not None else eng.tensor_copy(lo, src)
                ins.then_inc(s_lo, 1)

        @block.tensor
        def _(eng):
            for blk in blocks:
                if blk[0] == "L0":
                    _, g, c, s, half = blk
                    i, n, size = g * T + c - 1, n0_of(g, c, s), P * SIZES[g]
                    if half == 0:
                        eng.wait_ge(s_lo, number["W0", g, c, s] + 1)
                    if c == 0:
                        for t in range(4 * half, 4 * half + 4):
                            j = 8 * s + t
                            if j % 2 == 0:
                                eng.wait_ge(s_lo, number["X", g, j // 2] + 1)
                            if j == 0 and g:
                                eng.wait_ge(s_low, g)
                            for m in (xh, xl):
                                ins = eng.matmul(acca[:, 0:size], a_view(n % R0)[:, t, :], m[:, j, 0:size],
                                                 start=(j == 0 and m is xh), stop=(j == T - 1 and m is xl))
                        if half == 1:
                            ins.then_inc(s_w0, 1)
                        continue
                    acc = acc0[i % BANKS][:, 0:size]
                    if s == 0 and half == 0 and i >= BANKS:
                        eng.wait_ge(s_ev0, i - BANKS + 1)
                    if s == BSLOT and half == 0:
                        if c == 1:
                            eng.wait_ge(s_lo, number["LOW", g] + 1)
                        for q in range(PAIRS[g]):
                            if c in (1, 9):
                                eng.wait_ge(s_lo, number["B", g, q, c // 8] + 1)
                            eng.matmul(acc[:, N2 * q:N2 * q + N2], bs[:, q, P * (c - 1):P * c],
                                       lows[:, N2 * q:N2 * q + N2], start=False, stop=False)
                    for t in range(2 * half, 2 * half + 2):
                        j = 4 * s + t
                        wh, wl = w0s[:, n % R0, 0, t, :], w0s[:, n % R0, 1, t, :]
                        for a, m in ((wh, xh), (wh, xl), (wl, xh)):
                            ins = eng.matmul(acc, a, m[:, j, 0:size], start=(j == 0 and a is wh and m is xh),
                                             stop=(j == T - 1 and a is wl))
                    if half == 1:
                        ins.then_inc(s_w0, 1)
                else:
                    _, b, kc, s = blk
                    i, n = b * C1 + kc, n1_of(b, kc, s)
                    acc = acc1[i % BANKS][:]
                    if s == 0 and i >= BANKS:
                        eng.wait_ge(s_ev1, i - BANKS + 1)
                    if kc == 0 and s % 2 == 0:
                        eng.wait_ge(s_lo, number["Y", b, s // 2] + 1)
                    eng.wait_ge(s_lo, number["W1", b, kc, s] + 1)
                    for t in range(2):
                        j = 2 * s + t
                        k = (4 * b + j // 4) % RY
                        ah, al = yh[:, k, j % 4, :], yl[:, k, j % 4, :]
                        wh, wl = w1h[:, n % R1, t, :], w1l[:, n % R1, t, :]
                        for a, m in ((ah, wh), (ah, wl), (al, wh)):
                            ins = eng.matmul(acc, a, m, start=(j == 0 and a is ah and m is wh),
                                             stop=(j == T - 1 and a is al))
                    ins.then_inc(s_w1, 1)


def x_rows(xt, g, i):
    if SIZES[g] == G:
        return xt[FIRST[g] // G, i]
    at = FIRST[g] % G // 2
    return xt[FIRST[g] // G, i].rearrange("p (t n) -> p t n", t=2)[:, :, N2 * at:N2 * at + N2]


def transfers(kind, index):
    if kind == "B":
        return 2
    return SIZES[index[0]] if kind == "W0" and index[1] == 0 else 1


def diag_blocks(kind, index):
    if kind == "W0":
        _, c, s = index
        return [((c - 1) % 4) * P] if c > 0 and (c - 1) // 4 == s else []
    if kind == "W1":
        _, kc, s = index
        return [512 * (t % 2) + P * (t % 4) for t in (2 * s, 2 * s + 1)] if s // 2 == kc else []
    return []


def kernel(x, itok_B_1_7, itok_B_1_14, L0_cond_weight, L0_cond_bias, L0_cond_lora_a_weights,
           L0_cond_lora_b_weights, L0_cond_scaling_factors, L1_cond_weight):
    import numpy as np
    import concourse.bacc as bacc
    from concourse.bass_utils import run_bass_kernel_spmd as run

    c = np.ascontiguousarray
    x = np.asarray(x)
    arrays = {
        "xt": c(x.reshape(NB // G, G * P, XI, 2, P).transpose(0, 2, 4, 3, 1)).reshape(NB // G, XI, P, 1024),
        "a0": c(np.asarray(L0_cond_lora_a_weights).reshape(NA, RANK, SA, 8, P).transpose(0, 2, 4, 3, 1))
        .reshape(NA, SA, P, 8 * RANK),
        "w0": c(np.asarray(L0_cond_weight).reshape(T, P, S0, 4, P).transpose(0, 2, 4, 3, 1)).reshape(T, S0, P, 512),
        "w1": c(np.asarray(L1_cond_weight).reshape(NW, C1, 512, S1, 2, P).transpose(0, 1, 3, 5, 4, 2))
        .reshape(NW, C1, S1, P, 1024),
        "bt": c(np.asarray(L0_cond_lora_b_weights).transpose(0, 2, 1)),
        "bias": c(np.asarray(L0_cond_bias).reshape(T, P).T),
        "ids": c(np.asarray(itok_B_1_14).reshape(1, NB)),
        "idsb": c(np.broadcast_to(np.asarray(itok_B_1_7).reshape(1, NB), (P, NB))),
        "ids0": c(np.asarray(itok_B_1_7).reshape(1, NB)),
        "half": c((np.arange(P)[:, None] % 32 // RANK == np.arange(NB)[None, :] % 2).astype(np.float32)),
        "scal": c(np.broadcast_to(np.asarray(L0_cond_scaling_factors).reshape(1, NA), (P, NA))),
        "eye": np.eye(P, dtype=np.float32),
    }
    nc = bacc.Bacc("TRN2", target_bir_lowering=False, num_devices=1)
    aps = {name: nc.dram_tensor(name, a.shape, mybir.dt.from_np(a.dtype), kind="ExternalInput").ap()
           for name, a in arrays.items()}
    o = nc.dram_tensor("out", (NB, P, T * P), F32, kind="ExternalOutput").ap()
    program(nc, **aps, out=o)
    r = run(nc, [arrays], core_ids=[0])
    return r.results[0]["out"]
```

```python
from contextlib import ExitStack

import concourse.bass as bass
from concourse import mybir

F32 = mybir.dt.float32
F32R = mybir.dt.float32r
I32 = mybir.dt.int32
ALU = mybir.AluOpType

P = 128
NB = 32
G = 4
NG = NB // G
NP = NB // 2
N2 = 2 * P
T = 16
NA = 8
RANK = 16
NW = 16
C0 = T + 1
S0 = 4
SA = 2
BSLOT = 3
C1 = 4
S1 = 16
XI = 8

R0 = 2
R1 = 3
RY = 8
RW = 6
RX = 4
BANKS = 3
NOUT = 2
LEAD = 12
LATE = 5
EARLY = 8


def n0_of(g, c, s):
    return g * (SA + T * S0) + (SA + (c - 1) * S0 if c else 0) + s


def n1_of(pair, kc, s):
    return (pair * C1 + kc) * S1 + s


def plan_blocks():
    blocks, carry = [], []
    for g in range(NG + 1):
        first = [("L0", g, c, s, h) for c in range(C0) for s in range(S0 if c else SA) for h in range(2)]
        pairs = range(2 * g - 2, 2 * g) if g else []
        second = [("L1", pair, kc, s) for pair in pairs for kc in range(C1) for s in range(S1)]
        alone, rest = (first[:2 * SA], first[2 * SA:]) if g < NG else ([], [])
        if g == 1:
            carry, second = second[:EARLY], second[EARLY:]
            alone, blocks = blocks[len(blocks) - EARLY + len(alone):] + alone, blocks[:len(blocks) - EARLY + len(alone)]
        for i in range(max(len(alone), len(carry))):
            blocks += alone[i:i + 1] + carry[i:i + 1]
        carry = second[len(second) - LATE:] if rest and LATE else []
        second = second[:len(second) - len(carry)]
        done = 0
        for i in range(len(rest)):
            blocks.append(rest[i])
            until = (i + 1) * len(second) // len(rest)
            blocks += second[done:until]
            done = until
        blocks += second[done:]
    return blocks


def plan_splits(first0, last0, first1, last1):
    splits = []

    def add(kind, index, free, need):
        splits.append((max(free + 0.5, need - LEAD), need, kind, index))

    for g in range(NG):
        for c in range(C0):
            for s in range(S0 if c else SA):
                n = n0_of(g, c, s)
                add("W0", (g, c, s), last0[n - R0] if n >= R0 else -1, first0[n] + (0 if c else 0.15))
        for i in range(XI):
            free = last0[n0_of(g - 1, T, 1 + 2 * (i // 4))] if g else -1
            add("X", (g, i), free, first0[n0_of(g, 0, i // 4)] + 0.01 * i)
        for q in range(2):
            at = last0[n0_of(g - 1, 10 + q, 0)] if g else last0[n0_of(0, 1, q)] + 0.1
            splits.append((at + 0.5, first0[n0_of(g, 1, BSLOT)], "B", (g, q, 0)))
            at = first0[n0_of(g, 3 + q, 0)]
            splits.append((at + 0.5, first0[n0_of(g, 9, BSLOT)], "B", (g, q, 1)))
    for pair in range(NP):
        g = pair // 2
        for kc in range(C1):
            for s in range(S1):
                n = n1_of(pair, kc, s)
                add("W1", (pair, kc, s), last1[n - R1] if n >= R1 else -1, first1[n])
        for u in range(8):
            made = last0[n0_of(g, 2 * u + 2, S0 - 1)] + 0.2
            v = 8 * pair + u - RY
            free = last1[n1_of(v // 8, C1 - 1, 2 * (v % 8) + 1)] if v >= 0 else -1
            need = first1[n1_of(pair, 0, 2 * u)]
            if g + 1 < NG:
                need = min(need, last0[n0_of(g + 1, 1 + 8 * (pair % 2), S0 - 1)] - 6 + 0.1 * u + LEAD)
            add("Y", (pair, u), max(made, free), need)
    splits.sort()
    return splits


def program(nc, xt, a0, w0, w1, bt, bias, row, col, seq, half, scal, eye, out):
    blocks = plan_blocks()
    first0, last0, first1, last1 = {}, {}, {}, {}
    for at, block in enumerate(blocks):
        if block[0] == "L0":
            n = n0_of(*block[1:4])
            first0.setdefault(n, at)
            last0[n] = at
        else:
            n = n1_of(*block[1:4])
            first1[n] = last1[n] = at
    splits = plan_splits(first0, last0, first1, last1)
    number = {(kind, *index): n for n, (_, _, kind, index) in enumerate(splits)}

    with ExitStack() as ctx:
        def sb(name, shape, dt=F32):
            return ctx.enter_context(nc.sbuf_tensor(name, shape, dt))

        def sem(name):
            return ctx.enter_context(nc.semaphore(name))

        xh = sb("xh", [P, T, G * P], F32R)
        xl = sb("xl", [P, T, G * P], F32R)
        ybuf = sb("ybuf", [P, T * G * P])
        yh = sb("yh", [P, RY, 2, 2, P], F32R)
        yl = sb("yl", [P, RY, 2, 2, P], F32R)
        w0s = sb("w0s", [P, R0, 2, 4, P], F32R)
        w1h = sb("w1h", [P, R1, 2, 512], F32R)
        w1l = sb("w1l", [P, R1, 2, 512], F32R)
        bs = sb("bs", [P, 2, T * P], F32R)
        lows = sb("lows", [P, G * P], F32R)
        wraw = sb("wraw", [P, RW, 1024])
        ost = sb("ost", [P, NOUT, 512])
        eye_s = sb("eye_s", [P, P])
        bias_s = sb("bias_s", [P, T])
        wide = ybuf[0:NB, 0:3 * P].rearrange("p (k n) -> p k n", k=3)
        key_row, before_s = ybuf[0:NB, 384:416], ybuf[0:NB, 416:448]
        seq_s, table = ybuf[0:NB, 448:481], ybuf[0:NB, 484:487]
        key_col, rank = ybuf[0:NB, 488:489], ybuf[0:NB, 490:491]
        row_i, col_i = ybuf[0:NB, 512:544].bitcast(I32), ybuf[0:NB, 544:546].bitcast(I32)
        sorted_f = sb("sorted_f", [P, 3, NB])
        order_i = sb("order_i", [1, 4, NB], I32)
        mask = sb("mask", [P, NB])
        part = sb("part", [P, NB])
        half_s = sb("half_s", [P, NB])
        scal_s = sb("scal_s", [P, NA])
        acc0 = [ctx.enter_context(nc.psum_tensor(f"acc0_{i}", [P, 512], F32)) for i in range(BANKS)]
        acc1 = [ctx.enter_context(nc.psum_tensor(f"acc1_{i}", [P, 512], F32)) for i in range(4)]

        acca = ctx.enter_context(nc.psum_tensor("acca", [P, 512], F32))

        s_const = sem("s_const")
        s_eye = sem("s_eye")
        s_ids = sem("s_ids")
        s_key = sem("s_key")
        s_put = sem("s_put")
        s_order = sem("s_order")
        s_blank = sem("s_blank")
        s_mask = sem("s_mask")
        s_wraw = [sem(f"s_wraw{i}") for i in range(RW + RX)]
        s_diag = sem("s_diag")
        s_hi = sem("s_hi")
        s_lo = sem("s_lo")
        s_w0 = sem("s_w0")
        s_w1 = sem("s_w1")
        s_ev0 = sem("s_ev0")
        s_low = sem("s_low")
        s_ev1 = sem("s_ev1")
        s_out = [sem(f"s_out{i}") for i in range(NOUT)]

        y_places = ybuf[:, :].rearrange("p (a o c n) -> p a o c n", a=2, o=8, c=2)

        def y_tile(g, o):
            return y_places[:, o // 8, o % 8] if g % 2 == 0 else y_places[:, :, o % 8, o // 8]

        def y_unit(pair, u):
            o1, o0, b1 = u // 4, 2 * (u % 4), pair % 2
            if pair // 2 % 2 == 0:
                v = y_places[:, o1, o0:o0 + 2, b1]
            else:
                v = y_places[:, b1, o0:o0 + 2, o1]
            return v.rearrange("p o (b t) -> p o b t", b=2)

        place, landed, before, diag_count = {}, {}, {}, {}
        ring = [(k, None) for k in range(RW)]
        arrived = [0] * (RW + RX)
        spare = number["Y", NP - 2, 7]
        diagonals = 0
        for n, (_, _, kind, index) in enumerate(splits):
            if kind == "Y":
                continue
            if len(ring) == RW and ring[0][1] is not None and ring[0][1] > spare:
                ring = [(RW + k, spare) for k in range(RX)] + ring
            place[n], before[n] = ring.pop(0)
            arrived[place[n]] += 16 * transfers(kind, index)
            landed[n] = arrived[place[n]]
            ring.append((place[n], n))
            if diag_blocks(kind, index):
                diagonals += 1
                diag_count[n] = diagonals

        def raw_of(n):
            kind = splits[n][2]
            if kind == "B":
                return wraw[0:2 * RANK, place[n], :]
            if place[n] >= RW:
                k = place[n] - RW
                return ybuf[:, 1024 * k:1024 * k + 1024]
            return wraw[:, place[n], 0:512 if kind == "W0" else 1024]

        def raw_sem(n):
            return s_wraw[place[n]]

        scalar_tasks, vector_tasks, stores = [], [], []
        for n, (key, _, kind, index) in enumerate(splits):
            scalar_tasks.append((key, n, "hi", index))
            vector_tasks.append((key, n, "lo", index))
        vector_tasks.append((3, 0, "mask", None))
        for g in range(NG):
            vector_tasks.append((last0[n0_of(g, 0, SA - 1)] + 0.6, g, "low", None))
            for o in range(T):
                vector_tasks.append((last0[n0_of(g, o + 1, S0 - 1)] + 0.6, g * T + o, "ev0", (g, o)))
        for i in range(NB * C1):
            at = last1[S1 * (i // 2) + S1 - 1] + 2 * (i % 2)
            scalar_tasks.append((at + 3.6, i, "ev1", None))
            stores.append((at + 6, i))
        scalar_tasks.sort(key=lambda t: t[:2])
        vector_tasks.sort(key=lambda t: t[:2])

        def load_order(eng, what, g):
            each, top = ((4, NB), (4, NW), (4, NA), (2, 2))[what]
            _, values = nc.values_load_multi_w_load_instructions(
                order_i[0:1, what, each * g:each * (g + 1)], engines=[eng.engine], min_val=0, max_val=top - 1)
            return values

        def load_flags(eng):
            _, values = nc.values_load_multi_w_load_instructions(
                order_i[0:1, 3, 0:NP], engines=[eng.engine], min_val=0, max_val=1)
            return values

        block = ctx.enter_context(nc.Block())

        @block.sync
        def _(eng):
            registers = {}

            def order(g, what):
                if (what, g) not in registers:
                    registers.pop((what, g - 3), None)
                    registers[what, g] = load_order(eng, what, g)
                return registers[what, g]

            eng.dma_start(row_i, row).then_inc(s_ids, 16)
            eng.dma_start(seq_s, seq).then_inc(s_ids, 16)
            eng.dma_start(col_i, col).then_inc(s_ids, 16)
            eng.dma_start(half_s[:], half).then_inc(s_const, 16)
            eng.dma_start(scal_s[:], scal).then_inc(s_const, 16)
            eng.dma_start(bias_s[:], bias).then_inc(s_const, 16)
            eng.dma_start(eye_s[:], eye).then_inc(s_eye, 16)
            eng.wait_ge(s_order, 3)
            eng.wait_ge(s_blank, 1)

            def store(i):
                pair, kc = i // 2 // C1, i // 2 % C1
                b = order(pair // 2, 0)[2 * (pair % 2) + i % 2]
                eng.wait_ge(s_ev1, i + 1)
                eng.dma_start(out[bass.ds(b, 1), :, kc * 512:(kc + 1) * 512].rearrange("a p n -> (a p) n"),
                              ost[:, i % NOUT, :]).then_inc(s_out[i % NOUT], 16)

            stored = 0
            for n in sorted(place):
                kind, index = splits[n][2:4]
                while before[n] is not None and stores[stored][0] <= splits[before[n]][0]:
                    store(stored)
                    stored += 1
                if before[n] is not None:
                    eng.wait_ge(s_lo, before[n] + 1)
                dst, done = raw_of(n), raw_sem(n)
                if kind == "W1":
                    pair, kc, s = index
                    g, p = pair // 2, 2 * (pair % 2)
                    for i in range(2):
                        src = w1[bass.ds(order(g, 1)[p + i], 1), kc, s].rearrange("a p n -> (a p) n")
                        cond = {"cond": order(g, 3)[p // 2], "cond_hint": False} if i else {}
                        eng.dma_start(dst[:, 512 * i:512 * i + 512], src, **cond).then_inc(done, 16)
                elif kind == "X":
                    g, i = index
                    src = xt[bass.ds(order(g, 0)[i % G], 1), i // G].rearrange("a p n -> (a p) n")
                    eng.dma_start(dst, src).then_inc(done, 16)
                elif kind == "B":
                    g, q, h = index
                    for i in range(2):
                        src = bt[bass.ds(order(g, 2)[2 * q + i], 1), :, h * 1024:(h + 1) * 1024]
                        eng.dma_start(dst[RANK * i:RANK * (i + 1)], src.rearrange("a r n -> (a r) n"))\
                            .then_inc(done, 16)
                elif index[1] == 0:
                    g, _, s = index
                    for b in range(G):
                        src = a0[bass.ds(order(g, 2)[b], 1), s].rearrange("a p n -> (a p) n")
                        eng.dma_start(dst[:, P * b:P * b + P], src).then_inc(done, 16)
                else:
                    g, c, s = index
                    eng.dma_start(dst, w0[c - 1, s]).then_inc(done, 16)
                    for what, own, at in ((2, g + 1, (4, 2)), (0, g + 1, (7, 0)), (1, g, (13, 0)), (3, g, (14, 2))):
                        if own < NG and (c, s) == at:
                            order(own, what)
            for i in range(stored, NB * C1):
                store(i)
            for k in range(NOUT):
                eng.wait_ge(s_out[k], 16 * (NB * C1 // NOUT))

        @block.gpsimd
        def _(eng):
            for k in range(RW):
                ins = eng.memset(wraw[:, k, 512:1024], 0.0)
            ins.then_inc(s_blank, 1)
            eng.wait_ge(s_eye, 16)
            for n in sorted(diag_count):
                kind, index = splits[n][2:4]
                eng.wait_ge(raw_sem(n), landed[n])
                for at in diag_blocks(kind, index):
                    v = raw_of(n)[:, at:at + P]
                    ins = eng.tensor_tensor(v, v, eye_s[:], ALU.add)
                ins.then_inc(s_diag, 1)

        def a_view(k):
            return w0s[:, k].rearrange("p h t n -> p (h t) n")

        def split_views(n):
            kind, index = splits[n][2:4]
            if kind == "X":
                h, b = index[1] // G, index[1] % G
                v = raw_of(n).rearrange("p (t n) -> p t n", t=8)
                hi, lo = (w[:, 8 * h:8 * h + 8, P * b:P * b + P] for w in (xh, xl))
            elif kind == "B":
                _, q, h = index
                src, dst = raw_of(n), bs[:, q, 1024 * h:1024 * (h + 1)]
                return ([(src, dst[0:32]), (src, dst[32:64])],
                        [(src, None, dst[96:128]), (src, dst[0:32], dst[64:96])])
            elif kind == "W0" and index[1] == 0:
                v = raw_of(n).rearrange("p (b t r) -> p t b r", t=8, r=RANK)
                dst = a_view(n0_of(*index) % R0).rearrange("p t (b r) -> p t b r", r=RANK)
                hi, lo = dst[:, :, 0:G], dst[:, :, G:2 * G]
            elif kind == "W0":
                k = n0_of(*index) % R0
                v, hi, lo = raw_of(n).rearrange("p (t n) -> p t n", t=4), w0s[:, k, 0], w0s[:, k, 1]
            elif kind == "W1":
                k = n1_of(*index) % R1
                v, hi, lo = raw_of(n).rearrange("p (t n) -> p t n", t=2), w1h[:, k], w1l[:, k]
            else:
                k = (8 * index[0] + index[1]) % RY
                v, hi, lo = y_unit(*index), yh[:, k], yl[:, k]
            return [(v, hi)], [(v, hi, lo)]

        @block.scalar
        def _(eng):
            eng.wait_ge(s_order, 3)
            for _, n, what, index in scalar_tasks:
                if what == "ev1":
                    if n >= NOUT:
                        eng.wait_ge(s_out[n % NOUT], 16 * (n // NOUT))
                    eng.wait_ge(s_w1, S1 * (n // 2 + 1))
                    eng.copy(ost[:, n % NOUT, :], acc1[n % 4][:]).then_inc(s_ev1, 1)
                    continue
                kind = splits[n][2]
                if kind in ("X", "B", "W0", "W1"):
                    if n in diag_count:
                        eng.wait_ge(s_diag, diag_count[n])
                    else:
                        eng.wait_ge(raw_sem(n), landed[n])
                if kind == "X" and index[0]:
                    eng.wait_ge(s_w0, n0_of(index[0] - 1, T, 1 + 2 * (index[1] // G)) + 1)
                elif kind == "W0" and n0_of(*index) >= R0:
                    eng.wait_ge(s_w0, n0_of(*index) - R0 + 1)
                elif kind == "W1" and n1_of(*index) >= R1:
                    eng.wait_ge(s_w1, n1_of(*index) - R1 + 1)
                elif kind == "Y":
                    pair, u = index
                    eng.wait_ge(s_ev0, pair // 2 * T + 2 * u + 2)
                    v = 8 * pair + u - RY
                    if v >= 0:
                        eng.wait_ge(s_w1, n1_of(v // 8, C1 - 1, 2 * (v % 8) + 1) + 1)
                if kind == "B" and index[0]:
                    eng.wait_ge(s_w0, n0_of(index[0] - 1, 8 + 8 * index[2], BSLOT) + 1)
                for src, hi in split_views(n)[0]:
                    ins = eng.copy(hi, src)
                ins.then_inc(s_hi, 1)

        @block.vector
        def _(eng):
            eng.wait_ge(s_ids, 48)
            eng.tensor_copy(table[:, 1:3], col_i).then_inc(s_key, 1)
            eng.tensor_copy(table[:, 0:1], seq_s[:, NB:NB + 1]).then_inc(s_key, 1)
            eng.scalar_tensor_tensor(out=key_row, in0=row_i, scalar=float(NB), in1=seq_s[:, 0:NB],
                                     op0=ALU.mult, op1=ALU.add).then_inc(s_key, 1)
            eng.scalar_tensor_tensor(out=key_col, in0=col_i[:, 0:1], scalar=float(NB),
                                     in1=seq_s[:, NB:NB + 1], op0=ALU.mult, op1=ALU.add).then_inc(s_key, 1)
            eng.wait_ge(s_key, 4)
            eng.tensor_scalar(before_s, key_row, key_col[:, 0:1], None, ALU.is_lt).then_inc(s_key, 1)
            eng.tensor_copy(wide, table.unsqueeze(2).to_broadcast([NB, 3, P])).then_inc(s_key, 1)
            eng.wait_ge(s_key, 6)
            eng.tensor_reduce(rank, before_s, mybir.AxisListType.X, ALU.add).then_inc(s_key, 1)
            eng.wait_ge(s_key, 7)
            eng.tensor_scalar(before_s, seq_s[:, 0:NB], rank[:, 0:1], None, ALU.is_equal).then_inc(s_key, 1)
            eng.wait_ge(s_put, 1)
            eng.tensor_copy(sorted_f[:].rearrange("p k b -> p (k b)"), acca[:, 0:3 * NB]).then_inc(s_order, 1)
            eng.wait_ge(s_order, 1)
            eng.tensor_copy(order_i[:, 0:3, :], sorted_f[0:1]).then_inc(s_order, 1)
            pairs = sorted_f[0:1, 1, :].rearrange("p (q two) -> p q two", two=2)
            eng.tensor_tensor(order_i[:, 3, 0:NP], pairs[:, :, 0], pairs[:, :, 1], ALU.not_equal)\
                .then_inc(s_order, 1)
            idsb_f = sorted_f[:, 2, :]
            for _, n, what, index in vector_tasks:
                if what == "mask":
                    eng.wait_ge(s_const, 48)
                    eng.tensor_scalar(mask[:], idsb_f, 0.0, scal_s[:, 0:1], ALU.is_equal, ALU.mult)\
                        .then_inc(s_mask, 1)
                    for a in range(1, NA):
                        eng.tensor_scalar(part[:], idsb_f, float(a), scal_s[:, a:a + 1], ALU.is_equal,
                                          ALU.mult).then_inc(s_mask, 1)
                        eng.wait_ge(s_mask, 2 * a)
                        eng.tensor_tensor(mask[:], mask[:], part[:], ALU.add).then_inc(s_mask, 1)
                        eng.wait_ge(s_mask, 2 * a + 1)
                    eng.tensor_tensor(mask[:], mask[:], half_s[:], ALU.mult).then_inc(s_mask, 1)
                    eng.wait_ge(s_mask, 2 * NA)
                    continue
                if what == "low":
                    eng.wait_ge(s_w0, n0_of(n, 0, SA - 1) + 1)
                    if n:
                        eng.wait_ge(s_w0, n0_of(n - 1, T, BSLOT) + 1)
                    for q in range(2):
                        b, at = G * n + 2 * q, N2 * q
                        for row, to in ((32 * q, 0), (32 * q, 64), (64 + 32 * q, 96)):
                            m = mask[row:row + 32, b:b + 2].unsqueeze(2).to_broadcast([32, 2, P])
                            acc = acca[row:row + 32, at:at + N2].rearrange("p (b t) -> p b t", b=2)
                            dst = lows[to:to + 32, at:at + N2].rearrange("p (b t) -> p b t", b=2)
                            ins = eng.tensor_tensor(dst, acc, m, ALU.mult)
                    ins.then_inc(s_low, 1)
                    eng.wait_ge(s_low, 2 * n + 1)
                    for b in range(G):
                        row, cols = 32 * (b // 2), slice(P * b, P * b + P)
                        ins = eng.scalar_tensor_tensor(
                            out=lows[32:64, cols], in0=acca[row:row + 32, cols],
                            scalar=mask[row:row + 32, G * n + b:G * n + b + 1], in1=lows[0:32, cols],
                            op0=ALU.mult, op1=ALU.subtract)
                    ins.then_inc(s_low, 1)
                    continue
                if what == "ev0":
                    g, o = index
                    eng.wait_ge(s_w0, n0_of(g, o + 1, S0 - 1) + 1)
                    if g and o % 8 == 0:
                        eng.wait_ge(s_lo, max(number["Y", 2 * g - 2 + o // 8, u] for u in range(8)) + 1)
                    acc = acc0[n % BANKS][:].rearrange("p (b n) -> p b n", b=2)
                    eng.tensor_scalar(y_tile(g, o), acc, bias_s[:, o:o + 1], None, ALU.add).then_inc(s_ev0, 1)
                    continue
                eng.wait_ge(s_hi, n + 1)
                for src, hi, lo in split_views(n)[1]:
                    ins = eng.tensor_tensor(lo, src, hi, ALU.subtract) if hi is not None else eng.tensor_copy(lo, src)
                ins.then_inc(s_lo, 1)

        @block.tensor
        def _(eng):
            eng.wait_ge(s_key, 8)
            for k in range(3):
                ins = eng.matmul(acca[:, NB * k:NB * (k + 1)], wide[:, k, :], before_s, start=True, stop=True)
            ins.then_inc(s_put, 1)
            eng.wait_ge(s_order, 3)
            differ = load_flags(eng)
            for blk in blocks:
                if blk[0] == "L0":
                    _, g, c, s, half = blk
                    i, n = g * T + c - 1, n0_of(g, c, s)
                    if half == 0:
                        eng.wait_ge(s_lo, number["W0", g, c, s] + 1)
                    if c == 0:
                        for t in range(4 * half, 4 * half + 4):
                            j = 8 * s + t
                            if j % 8 == 0:
                                eng.wait_ge(s_lo, max(number["X", g, j // 2 + b] for b in range(G)) + 1)
                            if j == 0 and g:
                                eng.wait_ge(s_low, 2 * g)
                            for m in (xh, xl):
                                ins = eng.matmul(acca[:], a_view(n % R0)[:, t, :], m[:, j, :],
                                                 start=(j == 0 and m is xh), stop=(j == T - 1 and m is xl))
                        if half == 1:
                            ins.then_inc(s_w0, 1)
                        continue
                    acc = acc0[i % BANKS][:]
                    if s == 0 and half == 0 and i >= BANKS:
                        eng.wait_ge(s_ev0, i - BANKS + 1)
                    if s == BSLOT and half == 0:
                        if c == 1:
                            eng.wait_ge(s_low, 2 * g + 2)
                        for q in range(2):
                            if c in (1, 9):
                                eng.wait_ge(s_lo, number["B", g, q, c // 8] + 1)
                            eng.matmul(acc[:, N2 * q:N2 * q + N2], bs[:, q, P * (c - 1):P * c],
                                       lows[:, N2 * q:N2 * q + N2], start=False, stop=False)
                    for t in range(2 * half, 2 * half + 2):
                        j = 4 * s + t
                        wh, wl = w0s[:, n % R0, 0, t, :], w0s[:, n % R0, 1, t, :]
                        for a, m in ((wh, xh), (wh, xl), (wl, xh)):
                            ins = eng.matmul(acc, a, m[:, j, :], start=(j == 0 and a is wh and m is xh),
                                             stop=(j == T - 1 and a is wl))
                    if half == 1:
                        ins.then_inc(s_w0, 1)
                else:
                    _, pair, kc, s = blk
                    i, n = pair * C1 + kc, n1_of(pair, kc, s)
                    if s == 0 and i >= 2:
                        eng.wait_ge(s_ev1, 2 * (i - 1))
                    if kc == 0 and s % 2 == 0:
                        eng.wait_ge(s_lo, number["Y", pair, s // 2] + 1)
                    eng.wait_ge(s_lo, number["W1", pair, kc, s] + 1)
                    k = (8 * pair + s // 2) % RY
                    for b in range(2):
                        acc = acc1[2 * (i % 2) + b][:]
                        ah, al = yh[:, k, s % 2, b, :], yl[:, k, s % 2, b, :]
                        if b == 0:
                            wh, wl = w1h[:, n % R1, 0, :], w1l[:, n % R1, 0, :]
                        else:
                            wh, wl = (w[:, n % R1, bass.ds(differ[pair], 1), :].rearrange("p a n -> p (a n)")
                                      for w in (w1h, w1l))
                        for a, m in ((ah, wh), (ah, wl), (al, wh)):
                            ins = eng.matmul(acc, a, m, start=(s == 0 and a is ah and m is wh),
                                             stop=(s == S1 - 1 and a is al))
                    ins.then_inc(s_w1, 1)


def transfers(kind, index):
    if kind == "W0":
        return G if index[1] == 0 else 1
    return {"X": 1, "B": 2, "W1": 2}[kind]


def diag_blocks(kind, index):
    if kind == "W0":
        _, c, s = index
        return [((c - 1) % 4) * P] if c > 0 and (c - 1) // 4 == s else []
    if kind == "W1":
        _, kc, s = index
        return [512 * i + P * (s % 4) for i in range(2)] if s // 4 == kc else []
    return []


def kernel(x, itok_B_1_7, itok_B_1_14, L0_cond_weight, L0_cond_bias, L0_cond_lora_a_weights,
           L0_cond_lora_b_weights, L0_cond_scaling_factors, L1_cond_weight):
    import numpy as np
    import concourse.bacc as bacc
    from concourse.bass_utils import run_bass_kernel_spmd as run

    c = np.ascontiguousarray
    x = np.asarray(x)
    arrays = {
        "xt": c(x.reshape(NB, P, 2, 8, P).transpose(0, 2, 4, 3, 1)).reshape(NB, 2, P, 8 * P),
        "a0": c(np.asarray(L0_cond_lora_a_weights).reshape(NA, RANK, SA, 8, P).transpose(0, 2, 4, 3, 1))
        .reshape(NA, SA, P, 8 * RANK),
        "w0": c(np.asarray(L0_cond_weight).reshape(T, P, S0, 4, P).transpose(0, 2, 4, 3, 1)).reshape(T, S0, P, 512),
        "w1": c(np.asarray(L1_cond_weight).reshape(NW, C1, 512, S1, P).transpose(0, 1, 3, 4, 2)),
        "bt": c(np.asarray(L0_cond_lora_b_weights).transpose(0, 2, 1)),
        "bias": c(np.asarray(L0_cond_bias).reshape(T, P).T),
        "row": c(np.broadcast_to(np.asarray(itok_B_1_14).reshape(1, NB), (NB, NB))),
        "col": c(np.stack([np.asarray(itok_B_1_14), np.asarray(itok_B_1_7)], axis=1)),
        "seq": c(np.hstack([np.tile(np.arange(NB), (NB, 1)), np.arange(NB)[:, None]]).astype(np.float32)),
        "half": c((np.arange(P)[:, None] % 32 // RANK == np.arange(NB)[None, :] % 2).astype(np.float32)),
        "scal": c(np.broadcast_to(np.asarray(L0_cond_scaling_factors).reshape(1, NA), (P, NA))),
        "eye": np.eye(P, dtype=np.float32),
    }
    nc = bacc.Bacc("TRN2", target_bir_lowering=False, num_devices=1)
    aps = {name: nc.dram_tensor(name, a.shape, mybir.dt.from_np(a.dtype), kind="ExternalInput").ap()
           for name, a in arrays.items()}
    o = nc.dram_tensor("out", (NB, P, T * P), F32, kind="ExternalOutput").ap()
    program(nc, **aps, out=o)
    r = run(nc, [arrays], core_ids=[0])
    return r.results[0]["out"]
```
